# Optimizing a Trainium2 kernel written in Bass

```python
import numpy as np
import jax
import jax.numpy as jnp

def _softmax(x, axis=-1):
    return jax.nn.softmax(x, axis=axis)
def _gelu(x):
    return jax.nn.gelu(x, approximate=True)
def _silu(x):
    return jax.nn.silu(x)
def _sigmoid(x):
    return jax.nn.sigmoid(x)
def _layernorm(x, axis=-1, eps=1e-5):
    m = jnp.mean(x, axis=axis, keepdims=True)
    v = jnp.var(x, axis=axis, keepdims=True)
    return (x - m) / jnp.sqrt(v + eps)
def _scatter_add(tgt, idx, src, axis=0):
    return tgt.at[idx].add(src)
def _segment_sum(src, seg, n):
    return jax.ops.segment_sum(src, seg, n)

kernel_name = 'mk_rec_standalone_d1_rec_124048'

def setup_inputs(seed: int = 0):
    np.random.seed(seed)
    _w = jnp.asarray
    def _rec_inputs():
        import jax
        import jax.numpy as jnp
        _rk = jax.random.key(seed)
        r_inputs = -0.0002422 + 0.999987 * jax.random.normal(jax.random.fold_in(_rk, 1), (16384, 50, 64), jnp.float32)
        r_domain_ids = jax.random.randint(jax.random.fold_in(_rk, 2), (16384,), 1, 9, jnp.int32)
        return r_inputs, r_domain_ids
    r_inputs, r_domain_ids = _rec_inputs()
    def _L0_rec_setup():
        import jax, jax.numpy as jnp
        import numpy as np
        B, F, E, H, D = (8192, 50, 64, 2, 8)
        HD = E // H
        EPS = 1e-06
        key = jax.random.key(seed)
        ks = jax.random.split(key, 8)
        std = 0.05
        inputs = jax.random.normal(ks[0], (B, F, E), jnp.float32)
        domain_ids = jax.random.randint(ks[1], (B,), 1, D + 1)
        W_Query_domains = jax.random.normal(ks[2], (D, E, E), jnp.float32) * std
        W_key = jax.random.normal(ks[3], (E, E), jnp.float32) * std
        W_Value = jax.random.normal(ks[4], (E, E), jnp.float32) * std
        W_Res = jax.random.normal(ks[5], (E, E), jnp.float32) * std
        ln_scale = jax.random.normal(ks[6], (D, E), jnp.float32) * std
        ln_bias = jax.random.normal(ks[7], (D, E), jnp.float32) * std
        return dict(inputs=inputs, domain_ids=domain_ids, W_Query_domains=W_Query_domains, W_key=W_key, W_Value=W_Value, W_Res=W_Res, ln_scale=ln_scale, ln_bias=ln_bias)
    _L0_rec_all = _L0_rec_setup()
    _L0_rec_in = {k: v for k, v in _L0_rec_all.items() if k in ('W_Query_domains', 'W_key', 'W_Value', 'W_Res', 'ln_scale', 'ln_bias', )}
    del _L0_rec_all

    return {
        "r_inputs": r_inputs,
        "r_domain_ids": r_domain_ids,
        "L0_rec_W_Query_domains": _L0_rec_in["W_Query_domains"],
        "L0_rec_W_key": _L0_rec_in["W_key"],
        "L0_rec_W_Value": _L0_rec_in["W_Value"],
        "L0_rec_W_Res": _L0_rec_in["W_Res"],
        "L0_rec_ln_scale": _L0_rec_in["ln_scale"],
        "L0_rec_ln_bias": _L0_rec_in["ln_bias"],
    }

def reference(r_inputs, r_domain_ids, L0_rec_W_Query_domains, L0_rec_W_key, L0_rec_W_Value, L0_rec_W_Res, L0_rec_ln_scale, L0_rec_ln_bias):
    import jax
    import jax.numpy as jnp
    def _L0_rec_ref(inputs, domain_ids, W_Query_domains, W_key, W_Value, W_Res, ln_scale, ln_bias):
        import jax, jax.numpy as jnp
        import numpy as np
        B, F, E, H, D = (8192, 50, 64, 2, 8)
        HD = E // H
        EPS = 1e-06
        b, f, e = inputs.shape
        idx = domain_ids - 1
        keys = jnp.einsum('bfe,eo->bfo', inputs, W_key)
        values = jnp.einsum('bfe,eo->bfo', inputs, W_Value)
        Wq = W_Query_domains[idx]
        querys = jnp.einsum('bfe,beo->bfo', inputs, Wq)
        q = querys.reshape(b, f, H, HD)
        k = keys.reshape(b, f, H, HD)
        v = values.reshape(b, f, H, HD)
        scores = jnp.einsum('bihd,bjhd->bhij', q, k) / np.sqrt(HD).astype(np.float32)
        attn = jax.nn.softmax(scores, axis=-1)
        out = jnp.einsum('bhij,bjhd->bihd', attn, v).reshape(b, f, e)
        out = out + jnp.einsum('bfe,eo->bfo', inputs, W_Res)
        out = jax.nn.relu(out)
        gamma = ln_scale[idx][:, None, :]
        beta = ln_bias[idx][:, None, :]
        mean = jnp.mean(out, axis=-1, keepdims=True)
        var = jnp.mean(jnp.square(out - mean), axis=-1, keepdims=True)
        out = (out - mean) * jax.lax.rsqrt(var + EPS) * gamma + beta
        return out

    y = _L0_rec_ref(r_inputs, r_domain_ids, L0_rec_W_Query_domains, L0_rec_W_key, L0_rec_W_Value, L0_rec_W_Res, L0_rec_ln_scale, L0_rec_ln_bias)
    return y


_drawn_inputs = setup_inputs


def setup_inputs(seed=0):
    import zlib

    import numpy as np

    out = dict(_drawn_inputs(seed))
    spreads = {}
    factors = {}
    for name, (base, spread) in spreads.items():
        noise = np.random.default_rng([zlib.crc32(name.encode()), seed]).standard_normal(out[name].shape)
        drawn = base * np.exp(spread * noise) if base else spread * noise
        out[name] = jnp.asarray(drawn.astype(out[name].dtype))
    for name, factor in factors.items():
        out[name] = (out[name] * factor).astype(out[name].dtype)
    return out
```

```python
from contextlib import ExitStack

import concourse.bass as bass
from concourse import mybir

ALU = mybir.AluOpType
ACT = mybir.ActivationFunctionType
F32 = mybir.dt.float32
I32 = mybir.dt.int32
AX_X = mybir.AxisListType.X

F, E, H, D = 50, 64, 2, 8
HD = E // H
EPS = 1e-6
P = 128
PC = 5
GS = 2 * PC
U = 5
ITS = 5
NP = PC * U * ITS
SB = 2 * NP
FI = F // ITS
TOK = 2 * F
W = PC * TOK
HW_ = W // 2
PIECE = FI * E
RING = 2 * NP
ROUND = float(3 << 22)
LUMPS = [(0, 4), (4, 3), (7, 3)]
BUF3 = [0, 1, 2, 0, 1]
AGO3 = [2, 2, 5, 3, 3]
OHB = 4
GQ = 4


def windows_to_spans(windows):
    edges = sorted({e for w in windows.values() for e in w})
    for lo, hi in zip(edges, edges[1:]):
        on = {n for n, (a, b) in windows.items() if a <= lo and hi <= b}
        if on:
            yield lo, hi, on


def over(eng, windows, body):
    for lo, hi, on in windows_to_spans(windows):
        if hi - lo == 1:
            body(lo, on)
        else:
            with eng.Fori(lo, hi) as t:
                body(t, on)


def ge(eng, sem, value):
    if isinstance(value, int) and value <= 0:
        return
    eng.wait_ge(sem, value)


def build(nc, x, ids, w_q, w_k, w_v, w_res, ln_scale, ln_bias, out):
    B = x.shape[0]
    C = B // P
    NBLK = -(-(B + D * (GS - 1)) // SB)
    SLOTS = NBLK * SB
    NG = SLOTS // GS
    NI = NBLK * ITS

    a_tab = nc.dram_tensor("a_scratch", [D, P, 2 * P], F32, kind="Internal").ap()
    gb_tab = nc.dram_tensor("gb_scratch", [D, 2 * E], F32, kind="Internal").ap()
    x_rows = x.rearrange("b (q f) e -> (b q) (f e)", q=ITS)
    out_rows = out.rearrange("b (q f) e -> (b q) (f e)", q=ITS)

    with ExitStack() as ctx:
        def sb(name, shape, dt=F32):
            return ctx.enter_context(nc.sbuf_tensor(name, shape, dt))

        def sem(name):
            return ctx.enter_context(nc.semaphore(name))

        ps_t, ps_s, ps_pt, ps_v, ps_av, ps_rt, ps_xt, ps_bk = (
            ctx.enter_context(nc.psum_tensor(n, [P, 512], F32))
            for n in ("ps_t", "ps_s", "ps_pt", "ps_v", "ps_av", "ps_rt", "ps_xt", "ps_bk"))

        a_banks = [(ps_av, ps_rt), (ps_xt, ps_bk)]

        ident = sb("ident", [P, P])
        perm_id = sb("perm_id", [P, P])
        wv = sb("wv", [P, E])
        wres = sb("wres", [P, P])
        vmask = sb("vmask", [P, 2])
        mhalf = sb("mhalf", [P, 2 * FI])
        idx_tab = sb("idx_tab", [P, NI * 2], I32)
        dom_tab = sb("dom_tab", [P, NBLK], I32)
        gdom = sb("gdom", [1, NG], I32)
        xin = sb("xin", [P, 2, FI, E])
        xint = sb("xint", [P, FI, 2, E])
        xt = sb("xt", [P, F, RING])
        xbd = sb("xbd", [P, 3, PC, 2, F])
        a_sb = sb("a_sb", [P, U, 2 * P])
        t_sb = sb("t_sb", [P, 3, PC, H, F])
        e_sb = sb("e_sb", [P, U, W])
        pt_sb = sb("pt_sb", [P, 3, W])
        vbd = sb("vbd", [P, U, PC, H, 2, HD])
        rt_sb = sb("rt_sb", [P, U, F, PC])
        yt = sb("yt", [P, F, RING])
        yst = sb("yst", [P, FI, NP])
        r_sb = sb("r_sb", [P, 2, FI, E])
        c_sb = sb("c_sb", [P, 2, FI, E])
        sq_sb = sb("sq_sb", [P, 2, FI, E])
        n_sb = sb("n_sb", [P, 2, FI, E])
        o_sb = sb("o_sb", [P, 2, FI, E])
        gb_sb = sb("gb_sb", [P, 2, E])
        mx = sb("mx", [P, U, 2 * PC])
        sm = sb("sm", [P, U, 2 * PC])
        rc = sb("rc", [P, U, 2 * PC])
        lsum = sb("lsum", [P, 2 * FI])
        lmean = sb("lmean", [P, 2 * FI])
        lsq = sb("lsq", [P, 2 * FI])
        lvar = sb("lvar", [P, 2 * FI])
        rstd = sb("rstd", [P, 2 * FI])
        x_idx = sb("x_idx", [P, 2], I32)
        o_idx = sb("o_idx", [P, 2], I32)
        g_idx = sb("g_idx", [P, 1], I32)

        ytf = yt[:, :, :].rearrange("p f r -> p (f r)")
        at = [0]

        def scratch(n, parts=P):
            at[0] += n
            assert at[0] <= F * RING
            return ytf[0:parts, at[0] - n:at[0]]

        ids_i = scratch(C).bitcast(I32)
        ids_f = scratch(C)
        ones = scratch(max(C, P))
        oneh = scratch(D * C).rearrange("p (d c) -> p d c", d=D)
        pre = scratch(D * C).rearrange("p (d c) -> p d c", d=D)
        pos_f = scratch(C)
        blk = scratch(C)
        rem = scratch(C)
        samp1 = scratch(C)
        p_of = scratch(C)
        ns_of = scratch(C)
        irow_all = scratch(max(P, 2 * NBLK))
        irow, irow2 = irow_all[:, 0:P], irow_all[:, 0:2 * NBLK]
        oh_p = [scratch(P) for _ in range(OHB)]
        oh_ns = [scratch(2 * NBLK) for _ in range(OHB)]
        upper = scratch(P)
        tot, cnt, q0, q1, q2, gend, base, b1 = (scratch(D) for _ in range(8))
        one8 = scratch(D)
        kf = scratch(NBLK)
        kd = scratch(NBLK)
        kd2 = scratch(NBLK)
        pcol = scratch(1)
        pdiv = scratch(1)
        pm_e = scratch(2 * NBLK)
        pm_f = scratch(2 * NBLK)
        pm5 = scratch(2 * NI)
        xtf = xt[:, :, :].rearrange("p f r -> p (f r)")
        ghk = xtf[0:1, 0:NG]
        gd1 = xtf[0:1, NG:2 * NG]
        gd2 = xtf[0:1, 2 * NG:3 * NG]
        o0 = 3 * NG
        wq_in = xtf[0:E, o0:o0 + D * E].rearrange("p (d o) -> p d o", d=D)
        wqt = xtf[0:E, o0 + D * E:o0 + 2 * D * E].rearrange("p (d o) -> p d o", d=D)
        wk_in = xtf[0:E, o0 + 2 * D * E:o0 + 2 * D * E + E]
        wkt = xtf[0:E, o0 + 2 * D * E + E:o0 + 2 * D * E + 2 * E]
        o0 += 2 * D * E + 2 * E
        a_st = xtf[:, o0:o0 + D * 2 * P].rearrange("p (d n) -> p d n", d=D)
        assert o0 + D * 2 * P <= F * RING

        names = """ids_in w_in wk_in_s wvr_in gb_in_s gb_done samp oh_done perm_mm pool_c
            dve_c act_c cnt_ps wt_ps a_ps a_wr setup_pool setup_dve setup_act
            x_in y_in o_out g_in
            t_mm s_mm rt_mm v_mm pt_mm av_mm xt_mm bk_mm
            t_ev rt_ev v_ev e_exp pt_ev xt_ev bk_ev sq_done
            xc_done xbd_done max_done sub_done sum_done rc_done y_add lsum_done lmean_done c_done lsq_done
            lvar_done n_done e_norm rstd_done x_idx_done o_idx_done g_idx_done pool_go gam_done o_done""".split()
        S = {n: sem(n) for n in names}
        a_in = [sem(f"a_in{u}") for u in range(U)]
        block = ctx.enter_context(nc.Block())

        XT, A_LOAD, FRONT, LAG = (0, NI), (4, NI + 4), (5, NI + 5), (6, NI + 6)
        YST, BK, LN, OUT = (10, NI + 10), (11, NI + 11), (12, NI + 12), (13, NI + 13)

        def lagged(on, u, lag):
            return ("lag" if u < lag else "front") in on

        def chunk(t, u, lag=0):
            return (t - 5) * U + (u - lag)

        @block.sync
        def _(sp):
            sp.dma_start(ids_i, ids.rearrange("(p c) -> p c", p=P)).then_inc(S["ids_in"], 16)
            sp.dma_start(wq_in, w_q.rearrange("d e o -> e d o")).then_inc(S["w_in"], 16)
            sp.dma_start(wk_in, w_k).then_inc(S["wk_in_s"], 16)
            sp.wait_ge(S["setup_pool"], 1)
            for s in range(2):
                sp.dma_start(wv[s * E:(s + 1) * E, :], w_v).then_inc(S["wvr_in"], 16)
                for h in range(H):
                    c0 = h * E + s * HD
                    sp.dma_start(wres[s * E:(s + 1) * E, c0:c0 + HD],
                                 w_res[:, h * HD:(h + 1) * HD]).then_inc(S["wvr_in"], 16)
            sp.dma_start(gb_sb[0:D, 0, :], ln_scale).then_inc(S["gb_in_s"], 16)
            sp.dma_start(gb_sb[0:D, 1, :], ln_bias).then_inc(S["gb_in_s"], 16)
            sp.wait_ge(S["gb_in_s"], 32)
            sp.dma_start(gb_tab, gb_sb[0:D, :, :].rearrange("d a e -> d (a e)")).then_inc(S["gb_done"], 16)
            sp.wait_ge(S["setup_act"], 1)
            sp.dma_start(a_tab.rearrange("d p n -> p d n"), a_st).then_inc(S["a_wr"], 16)
            sp.wait_ge(S["a_wr"], 16)
            sp.wait_ge(S["gb_done"], 16)
            sp.wait_ge(S["setup_dve"], 1)

            def body(t, on):
                for u in range(U):
                    if "a" in on:
                        c = (t - 4) * U + u
                        if "a_wait" in on:
                            sp.wait_ge(S["t_mm"], c - U + 1)
                        d = sp.value_load(gdom[0:1, bass.ds(c, 1)], min_val=0, max_val=D - 1)
                        sp.dma_start(a_sb[:, u, :], a_tab[bass.ds(d, 1), :, :].rearrange("a p n -> p (a n)")
                                     ).then_inc(a_in[u], 16)
                    if u == U - 1 and "yst" in on:
                        j = t - 10
                        sp.wait_ge(S["y_add"], NI * U if "late" in on else (t - 5) * U)
                        if "yst_wait" in on:
                            sp.wait_ge(S["bk_mm"], j * 3)
                        sp.dma_start(yst[:, :, :], yt[:, bass.ds(j % ITS * FI, FI),
                                                      bass.ds(j // ITS % 2 * NP, NP)]).then_inc(S["y_in"], 16)

            over(sp, {"first": (0, 1), "a": A_LOAD, "a_wait": (5, NI + 4), "yst_wait": (11, NI + 10), "yst": YST, "late": (NI + 5, NI + 10)}, body)

        @block.gpsimd
        def _(pool):
            n = [0]

            def link(ins):
                n[0] += 1
                ins.then_inc(S["pool_c"], 1)
                pool.wait_ge(S["pool_c"], n[0])

            link(nc.gpsimd.memset(wres[:, :], 0.0))
            nc.gpsimd.memset(xbd[:, :, :, :, :], 0.0).then_inc(S["setup_pool"], 1)
            link(nc.gpsimd.memset(ident[:, :], 0.0))
            link(nc.gpsimd.affine_select(out=ident[:, :], in_=ident[:, :], compare_op=ALU.not_equal, fill=1.0,
                                         base=0, pattern=[[-1, P]], channel_multiplier=1))
            link(nc.gpsimd.memset(upper, 0.0))
            link(nc.gpsimd.affine_select(out=upper, in_=upper, compare_op=ALU.is_ge, fill=1.0,
                                         base=0, pattern=[[-1, P]], channel_multiplier=1))
            link(nc.gpsimd.iota(samp1, pattern=[[1, C]], base=1, channel_multiplier=C,
                                allow_small_or_imprecise_dtypes=True))
            link(nc.gpsimd.iota(irow_all, pattern=[[1, max(P, 2 * NBLK)]], base=0, channel_multiplier=0,
                                allow_small_or_imprecise_dtypes=True))
            link(nc.gpsimd.iota(pcol, pattern=[[0, 1]], base=0, channel_multiplier=1,
                                allow_small_or_imprecise_dtypes=True))
            link(nc.gpsimd.iota(kf, pattern=[[U * ITS, NBLK]], base=0, channel_multiplier=0,
                                allow_small_or_imprecise_dtypes=True))
            link(nc.gpsimd.iota(ghk, pattern=[[1, NG]], base=0, channel_multiplier=0,
                                allow_small_or_imprecise_dtypes=True))
            link(nc.gpsimd.memset(mhalf[:, :], -0.5))
            link(nc.gpsimd.memset(xin[:, :, :, :], 0.0))
            link(nc.gpsimd.memset(o_sb[:, :, :, :], 0.0))
            nc.gpsimd.memset(a_st, 0.0).then_inc(S["setup_pool"], 1)
            pool.wait_ge(S["setup_dve"], 2)

            def gather_x(t):
                nc.gpsimd.tensor_copy(x_idx[:, :], idx_tab[:, bass.ds(t * 2, 2)]).then_inc(S["x_idx_done"], 1)
                pool.wait_ge(S["x_idx_done"], t + 1)
                pool.sem_inc(S["pool_go"], 1)
                for s in range(2):
                    pool.indirect_dma_start(
                        xin[:, s, :, :].rearrange("p f e -> p (f e)"), None, x_rows,
                        bass.IndirectOffsetOnAxis(x_idx[:, s:s + 1], 0),
                        bounds_check=B * ITS - 1, oob_is_err=False).then_inc(S["x_in"], 16)

            def gather_gb(k):
                nc.gpsimd.tensor_copy(g_idx[:, :], dom_tab[:, bass.ds(k // ITS, 1)]).then_inc(S["g_idx_done"], 1)
                pool.wait_ge(S["g_idx_done"], k + 1)
                pool.sem_inc(S["pool_go"], 1)
                pool.indirect_dma_start(gb_sb[:, :, :].rearrange("p a e -> p (a e)"), None, gb_tab,
                                        bass.IndirectOffsetOnAxis(g_idx[:, :], 0)).then_inc(S["g_in"], 16)

            def body(t, on):
                if "x0" in on:
                    gather_x(0)
                for u in range(U):
                    if lagged(on, u, 2):
                        c, b = chunk(t, u, 2), (u - 2) % U
                        pool.wait_ge(S["rc_done"], c + 1)
                        v = e_sb[0:TOK, b, :].rearrange("p (g j) -> p g j", j=F)
                        r = rc[0:TOK, b, :].rearrange("p (g a) -> p g a", a=1).to_broadcast([TOK, 2 * PC, F])
                        nc.gpsimd.tensor_tensor(v, v, r, ALU.mult).then_inc(S["e_norm"], 1)
                    if "out" in on and u < GQ:
                        k = t - 13
                        g = 2 * FI // GQ
                        nv, ov = (a[0:NP, :, :, :].rearrange("p s f e -> p (s f) e")[:, u * g:(u + 1) * g, :]
                                  for a in (n_sb, o_sb))
                        if u == 0:
                            pool.wait_ge(S["n_done"], k + 1)
                            pool.wait_ge(S["g_in"], (k + 1) * 16)
                        gam, bet = (gb_sb[0:NP, a:a + 1, :].to_broadcast([NP, g, E]) for a in (0, 1))
                        nc.gpsimd.tensor_tensor(nv, nv, gam, ALU.mult).then_inc(S["gam_done"], 1)
                        if u == 0:
                            ge(pool, S["o_out"], k * 32)
                        pool.wait_ge(S["gam_done"], k * GQ + u + 1)
                        nc.gpsimd.tensor_tensor(ov, nv, bet, ALU.add).then_inc(S["o_done"], 1)
                        if u == GQ - 1:
                            nc.gpsimd.tensor_copy(o_idx[:, :], idx_tab[:, bass.ds(k * 2, 2)]
                                                  ).then_inc(S["o_idx_done"], 1)
                            pool.wait_ge(S["o_idx_done"], k + 1)
                            pool.wait_ge(S["o_done"], (k + 1) * GQ)
                            pool.sem_inc(S["pool_go"], 1)
                            for s in range(2):
                                pool.indirect_dma_start(
                                    out_rows, bass.IndirectOffsetOnAxis(o_idx[:, s:s + 1], 0),
                                    o_sb[:, s, :, :].rearrange("p f e -> p (f e)"), None,
                                    bounds_check=B * ITS - 1, oob_is_err=False).then_inc(S["o_out"], 16)
                    if u == 2 and "ln" in on:
                        k = t - 12
                        pool.wait_ge(S["lvar_done"], k + 1)
                        nc.gpsimd.tensor_tensor(rstd[0:NP, :], lvar[0:NP, :], mhalf[0:NP, :], ALU.pow
                                                ).then_inc(S["rstd_done"], 1)
                    if u == 1 and "x" in on:
                        pool.wait_ge(S["xc_done"], t + 1)
                        gather_x(t + 1)
                    if u == U - 1 and "gb" in on:
                        gather_gb(t - 12)

            over(pool, {"x0": (0, 1), "seventh": (6, 7), "x": (0, NI - 1), "front": FRONT, "lag": LAG, "ln": LN, "gb": (12, NI + 12),
                        "out": OUT}, body)
            pool.wait_ge(S["o_out"], NI * 32)

        @block.vector
        def _(dve):
            n = [0]

            def link(ins):
                n[0] += 1
                ins.then_inc(S["dve_c"], 1)
                dve.wait_ge(S["dve_c"], n[0])

            dve.wait_ge(S["ids_in"], 16)
            link(nc.vector.tensor_copy(ids_f, ids_i))
            link(nc.vector.memset(ones, 1.0))
            link(nc.vector.memset(one8, 1.0))
            for d in range(D):
                link(nc.vector.tensor_scalar(oneh[:, d, :], ids_f, float(d + 1), None, ALU.is_equal))
            for d in range(D):
                link(nc.vector.tensor_tensor_scan(pre[:, d, :], ones[:, 0:C], oneh[:, d, :], 0.0,
                                                  ALU.mult, ALU.add))
            nc.vector.tensor_copy(tot.rearrange("p (d a) -> p d a", a=1), pre[:, :, C - 1:C]
                                  ).then_inc(S["samp"], 1)
            dve.wait_ge(S["cnt_ps"], 1)
            link(nc.vector.tensor_copy(cnt, ps_s[:, D:2 * D]))
            link(nc.vector.tensor_scalar(q0, cnt, 1.0 / GS, 0.5 - 0.5 / GS, ALU.mult, ALU.add))
            link(nc.vector.tensor_scalar(q1, q0, ROUND, None, ALU.add))
            link(nc.vector.tensor_scalar(q2, q1, ROUND, None, ALU.subtract))
            link(nc.vector.tensor_tensor_scan(gend, one8, q2, 0.0, ALU.mult, ALU.add))
            link(nc.vector.tensor_tensor(base, gend, q2, ALU.subtract))
            link(nc.vector.tensor_scalar(b1, base, float(GS), -1.0, ALU.mult, ALU.add))
            link(nc.vector.tensor_tensor(base, b1, ps_s[:, 0:D], ALU.add))
            for d in range(D):
                link(nc.vector.scalar_tensor_tensor(out=oneh[:, d, :], in0=pre[:, d, :], scalar=base[:, d:d + 1],
                                                    in1=oneh[:, d, :], op0=ALU.add, op1=ALU.mult))
            link(nc.vector.tensor_reduce(out=pos_f, in_=oneh.rearrange("p d c -> p c d"), axis=AX_X, op=ALU.add))
            link(nc.vector.tensor_scalar(rem, pos_f, 1.0 / SB, -0.5 + 0.5 / SB, ALU.mult, ALU.add))
            link(nc.vector.tensor_scalar(blk, rem, ROUND, None, ALU.add))
            link(nc.vector.tensor_scalar(ids_f, blk, ROUND, None, ALU.subtract))
            link(nc.vector.scalar_tensor_tensor(out=rem, in0=ids_f, scalar=-float(SB), in1=pos_f,
                                                op0=ALU.mult, op1=ALU.add))
            link(nc.vector.tensor_scalar(blk, rem, 0.5, -0.25, ALU.mult, ALU.add))
            link(nc.vector.tensor_scalar(pos_f, blk, ROUND, None, ALU.add))
            link(nc.vector.tensor_scalar(p_of, pos_f, ROUND, None, ALU.subtract))
            link(nc.vector.scalar_tensor_tensor(out=pos_f, in0=p_of, scalar=-2.0, in1=rem,
                                                op0=ALU.mult, op1=ALU.add))
            link(nc.vector.scalar_tensor_tensor(out=ns_of, in0=ids_f, scalar=2.0, in1=pos_f,
                                                op0=ALU.mult, op1=ALU.add))
            dve.wait_ge(S["setup_pool"], 2)

            def one_hot(i, first):
                for b in range(OHB):
                    c = i * OHB + b
                    if not first:
                        dve.wait_ge(S["perm_mm"], c - OHB + 1)
                    nc.vector.tensor_scalar(oh_p[b], irow, p_of[:, bass.ds(c, 1)], None, ALU.is_equal)
                    nc.vector.tensor_scalar(oh_ns[b], irow2, ns_of[:, bass.ds(c, 1)], samp1[:, bass.ds(c, 1)],
                                            ALU.is_equal, ALU.mult).then_inc(S["oh_done"], 1)

            one_hot(0, True)
            with dve.Fori(1, C // OHB) as i:
                one_hot(i, False)

            def domains(k, a, b, parts):
                src = None
                for d in range(D - 1):
                    dst = (a, b)[d % 2]
                    if d == 0:
                        link(nc.vector.tensor_scalar(dst, k, gend[0:parts, 0:1], None, ALU.is_ge))
                    else:
                        link(nc.vector.scalar_tensor_tensor(out=dst, in0=k, scalar=gend[0:parts, d:d + 1], in1=src,
                                                            op0=ALU.is_ge, op1=ALU.add))
                    src = dst
                return src

            g = domains(ghk, gd1, gd2, 1)
            nc.vector.tensor_copy(gdom[:, :], g).then_inc(S["setup_dve"], 1)
            link(nc.vector.tensor_scalar(pdiv, pcol, 1.0 / PC, -0.5 + 0.5 / PC, ALU.mult, ALU.add))
            link(nc.vector.tensor_scalar(pcol, pdiv, ROUND, None, ALU.add))
            link(nc.vector.tensor_scalar(pdiv, pcol, ROUND, None, ALU.subtract))
            link(nc.vector.tensor_scalar(kf, kf, pdiv, None, ALU.add))
            g = domains(kf, kd, kd2, P)
            link(nc.vector.tensor_copy(dom_tab[:, :], g))
            dve.wait_ge(S["setup_pool"], 2)
            link(nc.vector.tensor_reduce(out=vmask[:, 0:1], in_=ident[:, 0:F], axis=AX_X, op=ALU.add))
            link(nc.vector.tensor_reduce(out=vmask[:, 1:2], in_=ident[:, F:P], axis=AX_X, op=ALU.add))
            link(nc.vector.tensor_copy(perm_id[:, :].rearrange("p (s h d) -> p s h d", s=2, h=H),
                                       ident[:, :].rearrange("p (h s d) -> p s h d", h=H, s=2)))
            dve.wait_ge(S["perm_mm"], C)
            link(nc.vector.tensor_scalar(pm_e, ps_av[:, 0:2 * NBLK], 0.0, float(B + 1), ALU.is_equal, ALU.mult))
            link(nc.vector.tensor_scalar(pm5[:, 0:2 * NBLK], ps_av[:, 0:2 * NBLK], 1.0, None, ALU.subtract))
            link(nc.vector.tensor_tensor(pm_f, pm5[:, 0:2 * NBLK], pm_e, ALU.add))
            tab = pm5.rearrange("p (n q s) -> p n q s", q=ITS, s=2)
            for q in range(ITS):
                link(nc.vector.tensor_scalar(tab[:, :, q, :], pm_f.rearrange("p (n s) -> p n s", s=2), float(ITS),
                                             float(q), ALU.mult, ALU.add))
            nc.vector.tensor_copy(idx_tab[:, :], pm5).then_inc(S["setup_dve"], 1)

            def body(t, on):
                k = t - 12
                for u in range(U):
                    if lagged(on, u, 5):
                        c, b = chunk(t, u, 5), u
                        dve.wait_ge(S["av_mm"], c + 1)
                        dve.wait_ge(S["rt_ev"], c + 1)
                        if u == 0 and "y_full" in on:
                            dve.wait_ge(S["y_in"], (t - 11) * 16)
                        off = chunk(t, u, 5) % (U * ITS * 2) * PC
                        for h in range(H):
                            r = slice(h * E, (h + 1) * E)
                            av = ps_av[r, 0:W].rearrange("p (q a i) -> p a i q", q=PC, a=H)[:, h, :, :]
                            last = nc.vector.tensor_tensor(yt[r, :, bass.ds(off, PC)], av, rt_sb[r, b, :, :], ALU.add)
                        last.then_inc(S["y_add"], 1)
                    if "front" in on:
                        c, b = chunk(t, u), BUF3[u]
                        if u == 0 and "xt_on" in on:
                            dve.wait_ge(S["xt_ev"], t * 3)
                        ge(dve, S["s_mm"], c - AGO3[u] + 1)
                        ge(dve, S["v_mm"], c - AGO3[u] + 1)
                        off = c % (U * ITS * 2) * PC
                        for s in range(2):
                            r = slice(s * E, (s + 1) * E)
                            last = nc.vector.tensor_copy(xbd[r, b, :, s, :].rearrange("p q f -> p f q"),
                                                         xt[r, :, bass.ds(off, PC)])
                        last.then_inc(S["xbd_done"], 1)
                    if lagged(on, u, 2):
                        c, b = chunk(t, u, 2), (u - 2) % U
                        dve.wait_ge(S["e_exp"], c + 1)
                        ge(dve, S["rc_done"], c - 4)
                        nc.vector.tensor_reduce(out=sm[0:TOK, b, :], in_=e_sb[0:TOK, b, :].rearrange(
                            "p (g j) -> p g j", j=F), axis=AX_X, op=ALU.add).then_inc(S["sum_done"], 1)
                    sv = ps_s[0:TOK, 0:W].rearrange("p (g j) -> p g j", j=F)
                    if lagged(on, u, 1):
                        c, b = chunk(t, u, 1), (u - 1) % U
                        dve.wait_ge(S["s_mm"], c + 1)
                        ge(dve, S["sub_done"], c - 4)
                        nc.vector.tensor_reduce(out=mx[0:TOK, b, :], in_=sv, axis=AX_X, op=ALU.max
                                                ).then_inc(S["max_done"], 1)
                    if lagged(on, u, 2):
                        c, b = chunk(t, u, 2), (u - 2) % U
                        dve.wait_ge(S["sum_done"], c + 1)
                        ge(dve, S["e_norm"], c - 4)
                        nc.vector.reciprocal(rc[0:TOK, b, :], sm[0:TOK, b, :]).then_inc(S["rc_done"], 1)
                    if lagged(on, u, 1):
                        c, b = chunk(t, u, 1), (u - 1) % U
                        dve.wait_ge(S["max_done"], c + 1)
                        ge(dve, S["pt_mm"], c - 4)
                        m = mx[0:TOK, b, :].rearrange("p (g a) -> p g a", a=1).to_broadcast([TOK, 2 * PC, F])
                        nc.vector.tensor_tensor(e_sb[0:TOK, b, :].rearrange("p (g j) -> p g j", j=F), sv, m,
                                                ALU.subtract).then_inc(S["sub_done"], 1)
                    if "ln" in on:
                        rv, cv, qv, nv = (a[0:NP, :, :, :].rearrange("p s f e -> p (s f) e")
                                          for a in (r_sb, c_sb, sq_sb, n_sb))

                        def wide(a):
                            return a[0:NP, :].rearrange("p (g a) -> p g a", a=1).to_broadcast([NP, 2 * FI, E])

                        if u == 0:
                            dve.wait_ge(S["bk_ev"], (k + 1) * 3)
                            nc.vector.tensor_reduce(out=lsum[0:NP, :], in_=rv, axis=AX_X, op=ALU.add
                                                    ).then_inc(S["lsum_done"], 1)
                            dve.wait_ge(S["lsum_done"], k + 1)
                            nc.vector.tensor_scalar(lmean[0:NP, :], lsum[0:NP, :], 1.0 / E, None, ALU.mult
                                                    ).then_inc(S["lmean_done"], 1)
                        if u == 1:
                            dve.wait_ge(S["lmean_done"], k + 1)
                            nc.vector.tensor_tensor(cv, rv, wide(lmean), ALU.subtract).then_inc(S["c_done"], 1)
                        if u == 2:
                            dve.wait_ge(S["sq_done"], k + 1)
                            nc.vector.tensor_reduce(out=lsq[0:NP, :], in_=qv, axis=AX_X, op=ALU.add
                                                    ).then_inc(S["lsq_done"], 1)
                            dve.wait_ge(S["lsq_done"], k + 1)
                            nc.vector.tensor_scalar(lvar[0:NP, :], lsq[0:NP, :], 1.0 / E, EPS, ALU.mult, ALU.add
                                                    ).then_inc(S["lvar_done"], 1)
                        if u == 4:
                            dve.wait_ge(S["rstd_done"], k + 1)
                            ge(dve, S["o_done"], k * GQ)
                            nc.vector.tensor_tensor(nv, cv, wide(rstd), ALU.mult).then_inc(S["n_done"], 1)

            over(dve, {"seventh": (6, 7), "y_full": (12, NI + 6), "front": FRONT, "lag": LAG, "xt_on": (0, NI + 1), "ln": LN}, body)

        @block.scalar
        def _(act):
            act.wait_ge(S["wt_ps"], 1)
            nc.scalar.activation(wqt.rearrange("p d o -> p (d o)"), ps_t[0:E, 0:D * E], ACT.Copy
                                 ).then_inc(S["act_c"], 1)
            nc.scalar.activation(wkt, ps_pt[0:E, 0:E], ACT.Copy, scale=float(HD) ** -0.5).then_inc(S["act_c"], 1)
            act.wait_ge(S["setup_pool"], 2)
            for d in range(D):
                act.wait_ge(S["a_ps"], d + 1)
                for s in range(2):
                    for h in range(H):
                        r = slice(s * E, (s + 1) * E)
                        last = nc.scalar.activation(a_st[r, d, h * P + s * E:h * P + (s + 1) * E],
                                                    a_banks[d % 2][h][r, 0:E], ACT.Copy)
                last.then_inc(S["act_c"], 1) if d < D - 1 else last.then_inc(S["setup_act"], 1)

            def body(t, on):
                j = t - 11
                for u in range(U):
                    if lagged(on, u, 4):
                        c, b = chunk(t, u, 4), BUF3[(u - 4) % U]
                        act.wait_ge(S["pt_mm"], c + 1)
                        ge(act, S["av_mm"], c - AGO3[(u - 4) % U] + 1)
                        nc.scalar.activation(pt_sb[0:TOK, b, :], ps_pt[0:TOK, 0:W], ACT.Copy).then_inc(S["pt_ev"], 1)
                    if "front" in on:
                        c, b = chunk(t, u), BUF3[u]
                        act.wait_ge(S["t_mm"], c + 1)
                        ge(act, S["s_mm"], c - AGO3[u] + 1)
                        nc.scalar.activation(t_sb[:, b, :, :, :],
                                             ps_t[:, 0:W].rearrange("p (h q i) -> p q h i", h=H, q=PC),
                                             ACT.Copy).then_inc(S["t_ev"], 1)
                    if lagged(on, u, 1):
                        c, b = chunk(t, u, 1), (u - 1) % U
                        act.wait_ge(S["v_mm"], c + 1)
                        ge(act, S["av_mm"], c - 4)
                        for s in range(2):
                            last = nc.scalar.activation(
                                vbd[0:TOK, b, :, :, s, :],
                                ps_v[0:TOK, 0:PC * E].rearrange("p (q h d) -> p q h d", q=PC, h=H),
                                ACT.Copy, scale=vmask[0:TOK, s:s + 1])
                        last.then_inc(S["v_ev"], 1)
                    if "front" in on:
                        c = chunk(t, u)
                        act.wait_ge(S["rt_mm"], c + 1)
                        ge(act, S["y_add"], c - 4)
                        nc.scalar.activation(rt_sb[:, u, :, :].rearrange("p f q -> p (f q)"), ps_rt[:, 0:HW_],
                                             ACT.Copy).then_inc(S["rt_ev"], 1)
                    if "xt" in on and 1 <= u <= 3:
                        f0, nf = LUMPS[u - 1]
                        act.wait_ge(S["xt_mm"], t * 3 + u)
                        if "lag" in on and u == 1:
                            act.wait_ge(S["t_mm"], (t - 5) * U)
                            act.wait_ge(S["rt_mm"], (t - 5) * U)
                            act.wait_ge(S["xbd_done"], (t - 5) * U)
                        nc.scalar.activation(
                            xt[:, bass.ds(t % ITS * FI + f0, nf), bass.ds(t // ITS % 2 * NP, NP)],
                            ps_xt[:, 0:nf * NP].rearrange("p (f q) -> p f q", f=nf), ACT.Copy
                        ).then_inc(S["xt_ev"], 1)
                    if "bk" in on and u >= 2:
                        f0, nf = LUMPS[u - 2]
                        act.wait_ge(S["bk_mm"], j * 3 + u - 1)
                        if u == 2:
                            ge(act, S["c_done"], j)
                        nc.scalar.activation(
                            r_sb[0:NP, :, f0:f0 + nf, :],
                            ps_bk[0:NP, 0:nf * P].rearrange("p (f s e) -> p s f e", f=nf, s=2),
                            ACT.Relu).then_inc(S["bk_ev"], 1)
                    if lagged(on, u, 1):
                        c, b = chunk(t, u, 1), (u - 1) % U
                        act.wait_ge(S["sub_done"], c + 1)
                        nc.scalar.activation(e_sb[0:TOK, b, :], e_sb[0:TOK, b, :], ACT.Exp).then_inc(S["e_exp"], 1)
                    if "xt" in on and u == 0:
                        act.wait_ge(S["x_in"], (t + 1) * 32)
                        ge(act, S["xt_mm"], t * 3)
                        nc.scalar.activation(xint[0:NP, :, :, :].rearrange("p f s e -> p s f e"), xin[0:NP, :, :, :],
                                             ACT.Copy).then_inc(S["xc_done"], 1)
                    if "ln" in on and u == 1:
                        k = t - 12
                        act.wait_ge(S["c_done"], k + 1)
                        ge(act, S["lsq_done"], k)
                        nc.scalar.activation(sq_sb[0:NP, :, :, :].rearrange("p s f e -> p (s f e)"),
                                             c_sb[0:NP, :, :, :].rearrange("p s f e -> p (s f e)"), ACT.Square
                                             ).then_inc(S["sq_done"], 1)

            over(act, {"first": (0, 1), "seventh": (6, 7), "xt": XT, "front": FRONT, "lag": LAG, "bk": BK, "ln": LN}, body)

        @block.tensor
        def _(pe):
            pe.wait_ge(S["setup_pool"], 2)
            pe.wait_ge(S["samp"], 1)
            nc.tensor.matmul(ps_s[:, 0:D], upper, tot, start=True, stop=True)
            nc.tensor.matmul(ps_s[:, D:2 * D], ones[:, 0:P], tot, start=True, stop=True).then_inc(S["cnt_ps"], 1)

            def place(i, first, stop):
                for b in range(OHB):
                    pe.wait_ge(S["oh_done"], i * OHB + b + 1)
                    nc.tensor.matmul(ps_av[:, 0:2 * NBLK], oh_p[b], oh_ns[b], start=first and b == 0,
                                     stop=stop and b == OHB - 1).then_inc(S["perm_mm"], 1)

            place(0, True, False)
            with pe.Fori(1, C // OHB - 1) as i:
                place(i, False, False)
            place(C // OHB - 1, False, True)
            pe.wait_ge(S["setup_dve"], 2)
            pe.wait_ge(S["w_in"], 16)
            pe.wait_ge(S["wk_in_s"], 16)
            for d in range(D):
                nc.tensor.transpose(ps_t[0:E, d * E:(d + 1) * E], wq_in[:, d, :], ident[0:E, 0:E])
            nc.tensor.transpose(ps_pt[0:E, 0:E], wk_in, ident[0:E, 0:E]).then_inc(S["wt_ps"], 1)
            pe.wait_ge(S["act_c"], 2)
            for d in range(D):
                if d >= 2:
                    pe.wait_ge(S["act_c"], d + 1)
                for s in range(2):
                    for h in range(H):
                        r = slice(h * HD, (h + 1) * HD)
                        last = nc.tensor.matmul(a_banks[d % 2][h][s * E:(s + 1) * E, 0:E], wqt[r, d, :], wkt[r, :],
                                                start=True, stop=True)
                last.then_inc(S["a_ps"], 1)
            pe.wait_ge(S["wvr_in"], 6 * 16)
            pe.wait_ge(S["setup_act"], 1)
            pe.wait_ge(S["a_wr"], 16)

            def body(t, on):
                j = t - 11
                for u in range(U):
                    if "front" in on:
                        c = chunk(t, u)
                        if u == 0 and "xt_on" in on:
                            pe.wait_ge(S["xt_ev"], t * 3)
                        off = c % (U * ITS * 2) * PC
                        pe.wait_ge(a_in[u], (t - 4) * 16)
                        ge(pe, S["t_ev"], c)
                        for h in range(H):
                            last = nc.tensor.matmul(ps_t[:, h * HW_:(h + 1) * HW_], a_sb[:, u, h * P:(h + 1) * P],
                                                    xt[:, :, bass.ds(off, PC)].rearrange("p f q -> p q f"),
                                                    start=True, stop=True)
                        last.then_inc(S["t_mm"], 1)
                    if lagged(on, u, 1):
                        c, b = chunk(t, u, 1), BUF3[(u - 1) % U]
                        pe.wait_ge(S["t_ev"], c + 1)
                        pe.wait_ge(S["xbd_done"], c + 1)
                        ge(pe, S["sub_done"], c)
                        for q in range(PC):
                            last = nc.tensor.matmul(
                                ps_s[0:TOK, q * TOK:(q + 1) * TOK],
                                t_sb[:, b, q, :, :].rearrange("p h i -> p (h i)"),
                                xbd[:, b, q, :, :].rearrange("p s j -> p (s j)"), start=True, stop=True)
                        last.then_inc(S["s_mm"], 1)
                    if lagged(on, u, 1):
                        c, b = chunk(t, u, 1), BUF3[(u - 1) % U]
                        ge(pe, S["v_ev"], c)
                        for q in range(PC):
                            last = nc.tensor.matmul(ps_v[0:TOK, q * E:(q + 1) * E],
                                                    xbd[:, b, q, :, :].rearrange("p s j -> p (s j)"), wv[:, :],
                                                    start=True, stop=True)
                        last.then_inc(S["v_mm"], 1)
                    if "front" in on:
                        c = chunk(t, u)
                        ge(pe, S["rt_ev"], c)
                        nc.tensor.matmul(ps_rt[:, 0:HW_], wres[:, :], xt[:, :, bass.ds(off, PC)],
                                         start=True, stop=True).then_inc(S["rt_mm"], 1)
                    if "xt" in on and 1 <= u <= 3:
                        f0, nf = LUMPS[u - 1]
                        if u == 1:
                            pe.wait_ge(S["xc_done"], t + 1)
                        ge(pe, S["xt_ev"], t * 3 + u - 1)
                        for f in range(nf):
                            last = nc.tensor.transpose(ps_xt[:, f * NP:(f + 1) * NP], xint[0:NP, f0 + f, :, :].rearrange("p s e -> p (s e)"),
                                                       ident[0:NP, 0:NP])
                        last.then_inc(S["xt_mm"], 1)
                    if "bk" in on and u >= 2:
                        f0, nf = LUMPS[u - 2]
                        if u == 2:
                            pe.wait_ge(S["y_in"], (j + 1) * 16)
                        ge(pe, S["bk_ev"], j * 3 + u - 2)
                        for f in range(nf):
                            last = nc.tensor.transpose(ps_bk[0:NP, f * P:(f + 1) * P], yst[:, f0 + f, :],
                                                       perm_id[:, :])
                        last.then_inc(S["bk_mm"], 1)
                    if lagged(on, u, 3):
                        c, b = chunk(t, u, 3), (u - 3) % U
                        pe.wait_ge(S["e_norm"], c + 1)
                        ge(pe, S["pt_ev"], c)
                        for q in range(PC):
                            last = nc.tensor.transpose(ps_pt[0:TOK, q * TOK:(q + 1) * TOK],
                                                       e_sb[0:TOK, b, q * TOK:(q + 1) * TOK], ident[0:TOK, 0:TOK])
                        last.then_inc(S["pt_mm"], 1)
                    if lagged(on, u, 4):
                        c, b = chunk(t, u, 4), (u - 4) % U
                        pe.wait_ge(S["pt_ev"], c + 1)
                        pe.wait_ge(S["v_ev"], c + 1)
                        ge(pe, S["y_add"], c)
                        for q in range(PC):
                            last = nc.tensor.matmul(
                                ps_av[:, q * TOK:(q + 1) * TOK],
                                vbd[0:TOK, b, q, :, :, :].rearrange("p h s d -> p (h s d)"),
                                pt_sb[0:TOK, BUF3[b], q * TOK:(q + 1) * TOK], start=True, stop=True)
                        last.then_inc(S["av_mm"], 1)

            over(pe, {"first": (0, 1), "seventh": (6, 7), "xt": XT, "front": FRONT, "lag": LAG, "bk": BK, "xt_on": (0, NI + 1)}, body)


_ARGS = [("r_inputs", "x"), ("r_domain_ids", "ids"), ("L0_rec_W_Query_domains", "w_q"), ("L0_rec_W_key", "w_k"),
         ("L0_rec_W_Value", "w_v"), ("L0_rec_W_Res", "w_res"), ("L0_rec_ln_scale", "ln_scale"),
         ("L0_rec_ln_bias", "ln_bias")]


def kernel(**inputs):
    import numpy as np
    import concourse.bacc as bacc
    from concourse.bass_utils import run_bass_kernel_spmd

    nc = bacc.Bacc("TRN2", target_bir_lowering=False, num_devices=1)
    arrays, args = {}, {}
    for name, short in _ARGS:
        a = np.ascontiguousarray(inputs[name])
        arrays[f"in_{short}"] = a
        args[short] = nc.dram_tensor(f"in_{short}", a.shape, mybir.dt.from_np(a.dtype), kind="ExternalInput").ap()
    shape = arrays["in_x"].shape
    args["out"] = nc.dram_tensor("out_y", shape, F32, kind="ExternalOutput").ap()
    build(nc, **args)
    r = run_bass_kernel_spmd(nc, [arrays], core_ids=[0])
    return r.results[0]["out_y"]
```

```python
from contextlib import ExitStack

import concourse.bass as bass
from concourse import mybir

ALU = mybir.AluOpType
ACT = mybir.ActivationFunctionType
F32 = mybir.dt.float32
F32R = mybir.dt.float32r
I32 = mybir.dt.int32
AX_X = mybir.AxisListType.X

F, E, H, D = 50, 64, 2, 8
HD = E // H
EPS = 1e-6
P = 128
PC = 5
GS = 2 * PC
U = 5
ITS = 5
NP = PC * U * ITS
SB = 2 * NP
FI = F // ITS
TOK = 2 * F
W = PC * TOK
HW_ = W // 2
RING = 2 * NP
ROUND = float(3 << 22)
XT_LUMPS = [(0, 4), (4, 3), (7, 3)]
BK_LUMPS = [(0, 3), (3, 3), (6, 4)]
BUF3 = [0, 1, 2, 0, 1]
AGO3 = [2, 2, 5, 3, 3]
NB3 = [2, 2, 1]
PARTS = [(0, 1), (1, 0), (0, 0)]
OHB = 4
GQ = 2


def windows_to_spans(windows):
    edges = sorted({e for w in windows.values() for e in w})
    for lo, hi in zip(edges, edges[1:]):
        on = {n for n, (a, b) in windows.items() if a <= lo and hi <= b}
        if on:
            yield lo, hi, on


def over(eng, windows, body):
    for lo, hi, on in windows_to_spans(windows):
        if hi - lo == 1:
            body(lo, on)
        else:
            with eng.Fori(lo, hi) as t:
                body(t, on)


def ge(eng, sem, value):
    if isinstance(value, int) and value <= 0:
        return
    eng.wait_ge(sem, value)


def build(nc, x, ids, w_q, w_k, w_v, w_res, ln_scale, ln_bias, out):
    B = x.shape[0]
    C = B // P
    NBLK = -(-(B + D * (GS - 1)) // SB)
    SLOTS = NBLK * SB
    NG = SLOTS // GS
    NI = NBLK * ITS

    gb_tab = nc.dram_tensor("gb_scratch", [D, 2 * E], F32, kind="Internal").ap()
    gb_pairs = nc.dram_tensor("gb_pairs", [NG, PC, 2 * E], F32, kind="Internal").ap()
    gb_rows = gb_pairs.rearrange("(n c) q e -> n (c q) e", n=NBLK)
    x_rows = x.rearrange("b (q f) e -> (b q) (f e)", q=ITS)
    out_rows = out.rearrange("b (q f) e -> (b q) (f e)", q=ITS)

    with ExitStack() as ctx:
        def sb(name, shape, dt=F32):
            return ctx.enter_context(nc.sbuf_tensor(name, shape, dt))

        def sem(name):
            return ctx.enter_context(nc.semaphore(name))

        ps_t, ps_s, ps_pt, ps_v, ps_av, ps_rt, ps_xt, ps_bk = (
            ctx.enter_context(nc.psum_tensor(n, [P, 512], F32))
            for n in ("ps_t", "ps_s", "ps_pt", "ps_v", "ps_av", "ps_rt", "ps_xt", "ps_bk"))

        a_banks = [(ps_av, ps_rt), (ps_xt, ps_bk)]

        ident = sb("ident", [P, P])
        perm_id = sb("perm_id", [P, P])
        wv = sb("wv", [P, E])
        a_tab = sb("a_tab", [P, D, 2, H, E], F32R)
        wres = sb("wres", [P, 2, P], F32R)
        vmask = sb("vmask", [P, 2])
        mhalf = sb("mhalf", [P, 1])
        idx_tab = sb("idx_tab", [P, NI * 2], I32)
        xin = sb("xin", [P, 2, FI, E])
        xint = sb("xint", [P, FI, 2, E])
        xt = sb("xt", [P, F, RING])
        xbd = sb("xbd", [P, 3, PC, 2, F])
        xh = sb("xh", [P, F, PC], F32R)
        xl = sb("xl", [P, F, PC], F32R)
        a_sb = sb("a_sb", [P, 3, 2, H, 2, E], F32R)
        t_sb = sb("t_sb", [P, 3, PC, H, F])
        e_sb = sb("e_sb", [P, U, W])
        gdom = e_sb[P - 1:P, :, :].rearrange("p u w -> p (u w)")[:, 0:NG].bitcast(I32)
        pt_sb = sb("pt_sb", [P, 3, W])
        vbd = sb("vbd", [P, U, PC, H, 2, HD])
        rt_sb = sb("rt_sb", [P, U, F, PC])
        yt = sb("yt", [P, F, RING])
        yst = sb("yst", [P, FI, NP])
        r_sb = sb("r_sb", [P, 2, FI, E])
        c_sb = sb("c_sb", [P, 2, FI, E])
        sq_sb = sb("sq_sb", [P, 2, FI, E])
        n_sb = sb("n_sb", [P, 2, FI, E])
        o_sb = sb("o_sb", [P, 2, FI, E])
        gb_sb = sb("gb_sb", [P, 2, E])
        mx = sb("mx", [P, U, 2 * PC])
        sm = sb("sm", [P, U, 2 * PC])
        lsum = sb("lsum", [P, 2 * FI])
        lsq = sb("lsq", [P, 2 * FI])
        lvar = sb("lvar", [P, 2 * FI])
        rstd = sb("rstd", [P, 2 * FI])
        x_idx = sb("x_idx", [P, 2], I32)
        o_idx = sb("o_idx", [P, 2], I32)

        ytf = yt[:, :, :].rearrange("p f r -> p (f r)")
        at = [0]

        def scratch(n, parts=P):
            at[0] += n
            assert at[0] <= F * RING
            return ytf[0:parts, at[0] - n:at[0]]

        ids_i = scratch(C).bitcast(I32)
        ids_f = scratch(C)
        ones = scratch(max(C, P))
        oneh = scratch(D * C).rearrange("p (d c) -> p d c", d=D)
        pre = scratch(D * C).rearrange("p (d c) -> p d c", d=D)
        pos_f = scratch(C)
        blk = scratch(C)
        rem = scratch(C)
        samp1 = scratch(C)
        p_of = scratch(C)
        ns_of = scratch(C)
        irow_all = scratch(max(P, 2 * NBLK))
        irow, irow2 = irow_all[:, 0:P], irow_all[:, 0:2 * NBLK]
        oh_p = [scratch(P) for _ in range(OHB)]
        oh_ns = [scratch(2 * NBLK) for _ in range(OHB)]
        upper = scratch(P)
        tot, cnt, q0, q1, q2, gend, base, b1 = (scratch(D) for _ in range(8))
        one8 = scratch(D)
        pm_e = scratch(2 * NBLK)
        pm_f = scratch(2 * NBLK)
        pm5 = scratch(2 * NI)
        xtf = xt[:, :, :].rearrange("p f r -> p (f r)")
        ghk = xtf[0:1, 0:NG]
        gd1 = xtf[0:1, NG:2 * NG]
        gd2 = xtf[0:1, 2 * NG:3 * NG]
        o0 = 3 * NG
        wq_in = xtf[0:E, o0:o0 + D * E].rearrange("p (d o) -> p d o", d=D)
        wqt = xtf[0:E, o0 + D * E:o0 + 2 * D * E].rearrange("p (d o) -> p d o", d=D)
        wk_in = xtf[0:E, o0 + 2 * D * E:o0 + 2 * D * E + E]
        wkt = xtf[0:E, o0 + 2 * D * E + E:o0 + 2 * D * E + 2 * E]
        o0 += 2 * D * E + 2 * E
        a_f32 = xtf[:, o0:o0 + D * H * E].rearrange("p (d h e) -> p d h e", d=D, h=H)
        o0 += D * H * E
        wres_f32 = xtf[:, o0:o0 + P]
        gdom_f = xtf[0:1, o0 + P:o0 + P + NG].bitcast(I32)
        assert TOK < P and NG <= U * W and o0 + P + NG <= F * RING

        names = """ids_in w_in wk_in_s wvr_in gb_in_s gb_done gdom_in samp oh_done perm_mm pool_c
            dve_c act_c cnt_ps wt_ps a_ps setup_pool setup_dve setup_act
            x_in y_in o_out g_in g_out
            t_mm s_mm rt_mm v_mm pt_mm av_mm xt_mm bk_mm
            t_ev rt_ev v_ev e_exp pt_ev xt_ev bk_ev sq_done
            xc_done xbd0_done xbd1_done xh_done xl_done max_done sub_done sum_done rc_done y_add
            lsum_done c_done lsq_done lvar_done n_done e_norm rstd_done x_idx_done o_idx_done pool_go
            gam_done o_done""".split()
        S = {n: sem(n) for n in names}
        a_in = [sem(f"a_in{b}") for b in range(3)]
        block = ctx.enter_context(nc.Block())

        XT, PRE, FRONT, LAG = (0, NI), (4, NI + 4), (5, NI + 5), (6, NI + 6)
        YST, BK, LN, OUT = (11, NI + 11), (11, NI + 11), (12, NI + 12), (13, NI + 13)

        def lagged(on, u, lag):
            if lag < 0:
                return ("front" if u < U + lag else "pre") in on
            return ("lag" if u < lag else "front") in on

        def chunk(t, u, lag=0):
            return (t - 5) * U + (u - lag)

        @block.sync
        def _(sp):
            sp.dma_start(ids_i, ids.rearrange("(p c) -> p c", p=P)).then_inc(S["ids_in"], 16)
            sp.dma_start(wq_in, w_q.rearrange("d e o -> e d o")).then_inc(S["w_in"], 16)
            sp.dma_start(wk_in, w_k).then_inc(S["wk_in_s"], 16)
            sp.wait_ge(S["setup_pool"], 1)
            for s in range(2):
                sp.dma_start(wv[s * E:(s + 1) * E, :], w_v).then_inc(S["wvr_in"], 16)
                for h in range(H):
                    c0 = h * E + s * HD
                    sp.dma_start(wres_f32[s * E:(s + 1) * E, c0:c0 + HD],
                                 w_res[:, h * HD:(h + 1) * HD]).then_inc(S["wvr_in"], 16)
            sp.dma_start(gb_sb[0:D, 0, :], ln_scale).then_inc(S["gb_in_s"], 16)
            sp.dma_start(gb_sb[0:D, 1, :], ln_bias).then_inc(S["gb_in_s"], 16)
            sp.wait_ge(S["gb_in_s"], 32)
            sp.dma_start(gb_tab, gb_sb[0:D, :, :].rearrange("d a e -> d (a e)")).then_inc(S["gb_done"], 16)
            sp.wait_ge(S["gb_done"], 16)
            sp.wait_ge(S["setup_dve"], 1)
            sp.dma_start(gdom, gdom_f).then_inc(S["gdom_in"], 16)
            sp.wait_ge(S["gdom_in"], 16)
            sp.wait_ge(S["setup_pool"], 2)
            sp.wait_ge(S["setup_dve"], 3)

            def body(t, on):
                for u in range(U):
                    if "front" in on:
                        c, b = chunk(t, u), BUF3[u]
                        ge(sp, S["t_mm"], c - AGO3[u] + 1)
                        d = sp.value_load(gdom[0:1, bass.ds(c, 1)], min_val=0, max_val=D - 1)
                        for s in range(2):
                            r = slice(s * E, (s + 1) * E)
                            sp.dma_start(a_sb[r, b, :, :, s, :].bitcast(F32),
                                         a_tab[r, bass.ds(d, 1), :, :, :].rearrange(
                                             "p a l h e -> p (a l) h e").bitcast(F32)
                                         ).then_inc(a_in[b], 16)
                        sp.dma_start(gb_pairs[bass.ds(c, 1), :, :], gb_tab[bass.ds(d, 1), :].rearrange(
                            "a (b e) -> a b e", b=1).to_broadcast([1, PC, 2 * E])).then_inc(S["g_out"], 16)
                    if u == 2 and "yst" in on:
                        j = t - 11
                        sp.wait_ge(S["y_add"], NI * U if "late" in on else (t - 6) * U)
                        if "yst_wait" in on:
                            sp.wait_ge(S["bk_mm"], j * 3)
                        sp.dma_start(yst[:, :, :], yt[:, bass.ds(j % ITS * FI, FI),
                                                      bass.ds(j // ITS % 2 * NP, NP)]).then_inc(S["y_in"], 16)

                    if u == U - 1 and "gb" in on:
                        k = t - 12
                        ge(sp, S["o_done"], k * GQ)
                        sp.wait_ge(S["g_out"], ((chunk(t, u) + 1) if "front" in on else NI * U) * 16)
                        sp.dma_start(gb_sb[0:NP, :, :].rearrange("p a e -> p (a e)"),
                                     gb_rows[bass.ds(k // ITS, 1), :, :].rearrange("a p e -> (a p) e")
                                     ).then_inc(S["g_in"], 16)

            over(sp, {"front": FRONT, "seventh": (6, 7), "yst": YST, "yst_wait": (12, NI + 11),
                      "late": (NI + 6, NI + 11), "gb": LN, "first ln": (12, 13)}, body)

        @block.gpsimd
        def _(pool):
            n = [0]

            def link(ins):
                n[0] += 1
                ins.then_inc(S["pool_c"], 1)
                pool.wait_ge(S["pool_c"], n[0])

            link(nc.gpsimd.memset(wres_f32, 0.0))
            nc.gpsimd.memset(xbd[:, :, :, :, :], 0.0).then_inc(S["setup_pool"], 1)
            link(nc.gpsimd.memset(ident[:, :], 0.0))
            link(nc.gpsimd.affine_select(out=ident[:, :], in_=ident[:, :], compare_op=ALU.not_equal, fill=1.0,
                                         base=0, pattern=[[-1, P]], channel_multiplier=1))
            link(nc.gpsimd.memset(upper, 0.0))
            link(nc.gpsimd.affine_select(out=upper, in_=upper, compare_op=ALU.is_ge, fill=1.0,
                                         base=0, pattern=[[-1, P]], channel_multiplier=1))
            link(nc.gpsimd.iota(samp1, pattern=[[1, C]], base=1, channel_multiplier=C,
                                allow_small_or_imprecise_dtypes=True))
            link(nc.gpsimd.iota(irow_all, pattern=[[1, max(P, 2 * NBLK)]], base=0, channel_multiplier=0,
                                allow_small_or_imprecise_dtypes=True))
            link(nc.gpsimd.iota(ghk, pattern=[[1, NG]], base=0, channel_multiplier=0,
                                allow_small_or_imprecise_dtypes=True))
            link(nc.gpsimd.memset(mhalf[:, :], -0.5))
            link(nc.gpsimd.memset(xin[:, :, :, :], 0.0))
            link(nc.gpsimd.memset(o_sb[:, :, :, :], 0.0))
            nc.gpsimd.memset(a_sb[:, :, :, :, :, :].bitcast(F32), 0.0).then_inc(S["setup_pool"], 1)
            pool.wait_ge(S["setup_dve"], 2)

            def gather_x(t):
                nc.gpsimd.tensor_copy(x_idx[:, :], idx_tab[:, bass.ds(t * 2, 2)]).then_inc(S["x_idx_done"], 1)
                pool.wait_ge(S["x_idx_done"], t + 1)
                pool.sem_inc(S["pool_go"], 1)
                for s in range(2):
                    pool.indirect_dma_start(
                        xin[:, s, :, :].rearrange("p f e -> p (f e)"), None, x_rows,
                        bass.IndirectOffsetOnAxis(x_idx[:, s:s + 1], 0),
                        bounds_check=B * ITS - 1, oob_is_err=False).then_inc(S["x_in"], 16)

            def body(t, on):
                if "x0" in on:
                    gather_x(0)
                for u in range(U):
                    if lagged(on, u, 2):
                        c, b = chunk(t, u, 2), (u - 2) % U
                        pool.wait_ge(S["rc_done"], c + 1)
                        v = e_sb[0:TOK, b, :].rearrange("p (g j) -> p g j", j=F)
                        r = sm[0:TOK, b, :].rearrange("p (g a) -> p g a", a=1).to_broadcast([TOK, 2 * PC, F])
                        nc.gpsimd.tensor_tensor(v, v, r, ALU.mult).then_inc(S["e_norm"], 1)
                    if "out" in on and u < GQ:
                        k = t - 13
                        g = 2 * FI // GQ
                        nv, ov = (a[0:NP, :, :, :].rearrange("p s f e -> p (s f) e")[:, u * g:(u + 1) * g, :]
                                  for a in (n_sb, o_sb))
                        if u == 0:
                            pool.wait_ge(S["n_done"], k + 1)
                            pool.wait_ge(S["g_in"], (k + 1) * 16)
                        gam, bet = (gb_sb[0:NP, a:a + 1, :].to_broadcast([NP, g, E]) for a in (0, 1))
                        nc.gpsimd.tensor_tensor(nv, nv, gam, ALU.mult).then_inc(S["gam_done"], 1)
                        if u == 0:
                            ge(pool, S["o_out"], k * 32)
                        pool.wait_ge(S["gam_done"], k * GQ + u + 1)
                        nc.gpsimd.tensor_tensor(ov, nv, bet, ALU.add).then_inc(S["o_done"], 1)
                    if "out" in on and u == GQ:
                        k = t - 13
                        nc.gpsimd.tensor_copy(o_idx[:, :], idx_tab[:, bass.ds(k * 2, 2)]
                                              ).then_inc(S["o_idx_done"], 1)
                        pool.wait_ge(S["o_idx_done"], k + 1)
                        pool.wait_ge(S["o_done"], (k + 1) * GQ)
                        pool.sem_inc(S["pool_go"], 1)
                        for s in range(2):
                            pool.indirect_dma_start(
                                out_rows, bass.IndirectOffsetOnAxis(o_idx[:, s:s + 1], 0),
                                o_sb[:, s, :, :].rearrange("p f e -> p (f e)"), None,
                                bounds_check=B * ITS - 1, oob_is_err=False).then_inc(S["o_out"], 16)
                    if u == 3 and "ln" in on:
                        k = t - 12
                        pool.wait_ge(S["lvar_done"], k + 1)
                        nc.gpsimd.tensor_tensor(rstd[0:NP, :], lvar[0:NP, :],
                                                mhalf[0:NP, :].to_broadcast([NP, 2 * FI]), ALU.pow
                                                ).then_inc(S["rstd_done"], 1)
                    if u == 4 and "x" in on:
                        pool.wait_ge(S["xc_done"], t + 1)
                        gather_x(t + 1)

            over(pool, {"x0": (0, 1), "seventh": (6, 7), "x": (0, NI - 1), "front": FRONT,
                        "lag": LAG, "ln": LN, "out": OUT, "first out": (13, 14)}, body)
            pool.wait_ge(S["o_out"], NI * 32)

        @block.vector
        def _(dve):
            n = [0]

            def link(ins):
                n[0] += 1
                ins.then_inc(S["dve_c"], 1)
                dve.wait_ge(S["dve_c"], n[0])

            dve.wait_ge(S["ids_in"], 16)
            link(nc.vector.tensor_copy(ids_f, ids_i))
            link(nc.vector.memset(ones, 1.0))
            link(nc.vector.memset(one8, 1.0))
            for d in range(D):
                link(nc.vector.tensor_scalar(oneh[:, d, :], ids_f, float(d + 1), None, ALU.is_equal))
            for d in range(D):
                link(nc.vector.tensor_tensor_scan(pre[:, d, :], ones[:, 0:C], oneh[:, d, :], 0.0,
                                                  ALU.mult, ALU.add))
            nc.vector.tensor_copy(tot.rearrange("p (d a) -> p d a", a=1), pre[:, :, C - 1:C]
                                  ).then_inc(S["samp"], 1)
            dve.wait_ge(S["cnt_ps"], 1)
            link(nc.vector.tensor_copy(cnt, ps_s[:, D:2 * D]))
            link(nc.vector.tensor_scalar(q0, cnt, 1.0 / GS, 0.5 - 0.5 / GS, ALU.mult, ALU.add))
            link(nc.vector.tensor_scalar(q1, q0, ROUND, None, ALU.add))
            link(nc.vector.tensor_scalar(q2, q1, ROUND, None, ALU.subtract))
            link(nc.vector.tensor_tensor_scan(gend, one8, q2, 0.0, ALU.mult, ALU.add))
            link(nc.vector.tensor_tensor(base, gend, q2, ALU.subtract))
            link(nc.vector.tensor_scalar(b1, base, float(GS), -1.0, ALU.mult, ALU.add))
            link(nc.vector.tensor_tensor(base, b1, ps_s[:, 0:D], ALU.add))
            for d in range(D):
                link(nc.vector.scalar_tensor_tensor(out=oneh[:, d, :], in0=pre[:, d, :], scalar=base[:, d:d + 1],
                                                    in1=oneh[:, d, :], op0=ALU.add, op1=ALU.mult))
            link(nc.vector.tensor_reduce(out=pos_f, in_=oneh.rearrange("p d c -> p c d"), axis=AX_X, op=ALU.add))
            link(nc.vector.tensor_scalar(rem, pos_f, 1.0 / SB, -0.5 + 0.5 / SB, ALU.mult, ALU.add))
            link(nc.vector.tensor_scalar(blk, rem, ROUND, None, ALU.add))
            link(nc.vector.tensor_scalar(ids_f, blk, ROUND, None, ALU.subtract))
            link(nc.vector.scalar_tensor_tensor(out=rem, in0=ids_f, scalar=-float(SB), in1=pos_f,
                                                op0=ALU.mult, op1=ALU.add))
            link(nc.vector.tensor_scalar(blk, rem, 0.5, -0.25, ALU.mult, ALU.add))
            link(nc.vector.tensor_scalar(pos_f, blk, ROUND, None, ALU.add))
            link(nc.vector.tensor_scalar(p_of, pos_f, ROUND, None, ALU.subtract))
            link(nc.vector.scalar_tensor_tensor(out=pos_f, in0=p_of, scalar=-2.0, in1=rem,
                                                op0=ALU.mult, op1=ALU.add))
            link(nc.vector.scalar_tensor_tensor(out=ns_of, in0=ids_f, scalar=2.0, in1=pos_f,
                                                op0=ALU.mult, op1=ALU.add))
            dve.wait_ge(S["setup_pool"], 2)

            def one_hot(i, first):
                for b in range(OHB):
                    c = i * OHB + b
                    if not first:
                        dve.wait_ge(S["perm_mm"], c - OHB + 1)
                    nc.vector.tensor_scalar(oh_p[b], irow, p_of[:, bass.ds(c, 1)], None, ALU.is_equal)
                    nc.vector.tensor_scalar(oh_ns[b], irow2, ns_of[:, bass.ds(c, 1)], samp1[:, bass.ds(c, 1)],
                                            ALU.is_equal, ALU.mult).then_inc(S["oh_done"], 1)

            one_hot(0, True)
            with dve.Fori(1, C // OHB) as i:
                one_hot(i, False)

            src = None
            for d in range(D - 1):
                dst = (gd1, gd2)[d % 2]
                if d == 0:
                    link(nc.vector.tensor_scalar(dst, ghk, gend[0:1, 0:1], None, ALU.is_ge))
                else:
                    link(nc.vector.scalar_tensor_tensor(out=dst, in0=ghk, scalar=gend[0:1, d:d + 1], in1=src,
                                                        op0=ALU.is_ge, op1=ALU.add))
                src = dst
            nc.vector.tensor_copy(gdom_f, src).then_inc(S["setup_dve"], 1)
            dve.wait_ge(S["setup_pool"], 2)
            link(nc.vector.tensor_reduce(out=vmask[:, 0:1], in_=ident[:, 0:F], axis=AX_X, op=ALU.add))
            link(nc.vector.tensor_reduce(out=vmask[:, 1:2], in_=ident[:, F:P], axis=AX_X, op=ALU.add))
            link(nc.vector.tensor_copy(perm_id[:, :].rearrange("p (s h d) -> p s h d", s=2, h=H),
                                       ident[:, :].rearrange("p (h s d) -> p s h d", h=H, s=2)))
            dve.wait_ge(S["perm_mm"], C)
            link(nc.vector.tensor_scalar(pm_e, ps_av[:, 0:2 * NBLK], 0.0, float(B + 1), ALU.is_equal, ALU.mult))
            link(nc.vector.tensor_scalar(pm5[:, 0:2 * NBLK], ps_av[:, 0:2 * NBLK], 1.0, None, ALU.subtract))
            link(nc.vector.tensor_tensor(pm_f, pm5[:, 0:2 * NBLK], pm_e, ALU.add))
            tab = pm5.rearrange("p (n q s) -> p n q s", q=ITS, s=2)
            for q in range(ITS):
                link(nc.vector.tensor_scalar(tab[:, :, q, :], pm_f.rearrange("p (n s) -> p n s", s=2), float(ITS),
                                             float(q), ALU.mult, ALU.add))
            nc.vector.tensor_copy(idx_tab[:, :], pm5).then_inc(S["setup_dve"], 1)
            dve.wait_ge(S["setup_act"], 1)
            link(nc.vector.tensor_tensor(a_tab[:, :, 1, :, :], a_f32, a_tab[:, :, 0, :, :].bitcast(F32), ALU.subtract))
            nc.vector.tensor_tensor(wres[:, 1, :], wres_f32, wres[:, 0, :].bitcast(F32), ALU.subtract
                                    ).then_inc(S["setup_dve"], 1)

            def row_sums(k, part):
                f = (slice(0, BK_LUMPS[0][1]), slice(BK_LUMPS[0][1], FI))[part]
                dve.wait_ge(S["bk_ev"], k * 3 + (1, 3)[part])
                ge(dve, S["c_done"], k)
                nc.vector.tensor_reduce(out=lsum[0:NP, :].rearrange("p (s f) -> p s f", s=2)[:, :, f],
                                        in_=r_sb[0:NP, :, f, :], axis=AX_X, op=ALU.add).then_inc(S["lsum_done"], 1)

            def body(t, on):
                k = t - 12
                for u in range(U):
                    if "front" in on:
                        ge(dve, S["s_mm"], chunk(t, u) - AGO3[u] + 1)
                        ge(dve, S["v_mm"], chunk(t, u) - AGO3[u] + 1)
                        if u == 0 and "xt_on" in on:
                            dve.wait_ge(S["xt_ev"], t * 3)
                    if lagged(on, u, 5):
                        c, b = chunk(t, u, 5), u
                        dve.wait_ge(S["av_mm"], c + 1)
                        dve.wait_ge(S["rt_ev"], c + 1)
                        if u == 0 and "y_full" in on:
                            dve.wait_ge(S["y_in"], (t - 11) * 16)
                        off = c % (U * ITS * 2) * PC
                        for h in range(H):
                            r = slice(h * E, (h + 1) * E)
                            av = ps_av[r, 0:W].rearrange("p (q a i) -> p a i q", q=PC, a=H)[:, h, :, :]
                            last = nc.vector.tensor_tensor(yt[r, :, bass.ds(off, PC)], av, rt_sb[r, b, :, :], ALU.add)
                        last.then_inc(S["y_add"], 1)
                    if "front" in on:
                        c, b = chunk(t, u), BUF3[u]
                        off = c % (U * ITS * 2) * PC
                        nc.vector.tensor_copy(xbd[0:E, b, :, 0, :].rearrange("p q f -> p f q"),
                                              xt[0:E, :, bass.ds(off, PC)]).then_inc(S["xbd0_done"], 1)
                    if lagged(on, u, 2):
                        c, b = chunk(t, u, 2), (u - 2) % U
                        dve.wait_ge(S["e_exp"], c + 1)
                        ge(dve, S["e_norm"], c - 4)
                        nc.vector.tensor_reduce(out=sm[0:TOK, b, :], in_=e_sb[0:TOK, b, :].rearrange(
                            "p (g j) -> p g j", j=F), axis=AX_X, op=ALU.add).then_inc(S["sum_done"], 1)
                    sv = ps_s[0:TOK, 0:W].rearrange("p (g j) -> p g j", j=F)
                    if lagged(on, u, 1):
                        c, b = chunk(t, u, 1), (u - 1) % U
                        dve.wait_ge(S["s_mm"], c + 1)
                        ge(dve, S["sub_done"], c - 4)
                        nc.vector.tensor_reduce(out=mx[0:TOK, b, :], in_=sv, axis=AX_X, op=ALU.max
                                                ).then_inc(S["max_done"], 1)
                    if lagged(on, u, 2):
                        c, b = chunk(t, u, 2), (u - 2) % U
                        dve.wait_ge(S["sum_done"], c + 1)
                        nc.vector.reciprocal(sm[0:TOK, b, :], sm[0:TOK, b, :]).then_inc(S["rc_done"], 1)
                    if lagged(on, u, 1):
                        c, b = chunk(t, u, 1), (u - 1) % U
                        dve.wait_ge(S["max_done"], c + 1)
                        ge(dve, S["pt_mm"], c - 4)
                        m = mx[0:TOK, b, :].rearrange("p (g a) -> p g a", a=1).to_broadcast([TOK, 2 * PC, F])
                        nc.vector.tensor_tensor(e_sb[0:TOK, b, :].rearrange("p (g j) -> p g j", j=F), sv, m,
                                                ALU.subtract).then_inc(S["sub_done"], 1)
                    if lagged(on, u, -1):
                        c = chunk(t, u, -1)
                        off = c % (U * ITS * 2) * PC
                        dve.wait_ge(S["xh_done"], c + 1)
                        ge(dve, S["rt_mm"], c)
                        nc.vector.tensor_tensor(xl[:, :, :], xt[:, :, bass.ds(off, PC)], xh[:, :, :].bitcast(F32),
                                                ALU.subtract).then_inc(S["xl_done"], 1)
                    if u == 3 and "bk" in on:
                        row_sums(t - 11, 0)
                    if "ln" in on:
                        rv, cv, qv, nv = (a[0:NP, :, :, :].rearrange("p s f e -> p (s f) e")
                                          for a in (r_sb, c_sb, sq_sb, n_sb))

                        def wide(a):
                            return a[0:NP, :].rearrange("p (g a) -> p g a", a=1).to_broadcast([NP, 2 * FI, E])

                        if u == 0:
                            row_sums(k, 1)
                        if u == 1:
                            dve.wait_ge(S["lsum_done"], (k + 1) * 2)
                            nc.vector.scalar_tensor_tensor(out=cv, in0=rv, scalar=float(E), in1=wide(lsum),
                                                           op0=ALU.mult, op1=ALU.subtract).then_inc(S["c_done"], 1)
                        if u == 2:
                            dve.wait_ge(S["sq_done"], k + 1)
                            nc.vector.tensor_reduce(out=lsq[0:NP, :], in_=qv, axis=AX_X, op=ALU.add
                                                    ).then_inc(S["lsq_done"], 1)
                            dve.wait_ge(S["lsq_done"], k + 1)
                            nc.vector.tensor_scalar(lvar[0:NP, :], lsq[0:NP, :], 1.0 / E, EPS * E * E, ALU.mult, ALU.add
                                                    ).then_inc(S["lvar_done"], 1)
                        if u == 4:
                            dve.wait_ge(S["rstd_done"], k + 1)
                            ge(dve, S["o_done"], k * GQ)
                            nc.vector.tensor_tensor(nv, cv, wide(rstd), ALU.mult).then_inc(S["n_done"], 1)

            over(dve, {"pre": PRE, "front": FRONT, "seventh": (6, 7), "lag": LAG, "xt_on": (0, NI + 1),
                       "y_full": (12, NI + 6), "bk": BK, "ln": LN, "first ln": (12, 13)}, body)

        @block.scalar
        def _(act):
            act.wait_ge(S["wt_ps"], 1)
            nc.scalar.activation(wqt.rearrange("p d o -> p (d o)"), ps_t[0:E, 0:D * E], ACT.Copy
                                 ).then_inc(S["act_c"], 1)
            nc.scalar.activation(wkt, ps_pt[0:E, 0:E], ACT.Copy, scale=float(HD) ** -0.5).then_inc(S["act_c"], 1)
            for d in range(D):
                act.wait_ge(S["a_ps"], d + 1)
                for s in range(2):
                    for h in range(H):
                        r = slice(s * E, (s + 1) * E)
                        last = nc.scalar.activation(a_f32[r, d, h, :], a_banks[d % 2][h][r, 0:E], ACT.Copy)
                last.then_inc(S["act_c"], 1)
            act.wait_ge(S["act_c"], 2 + D)
            act.wait_ge(S["wvr_in"], 6 * 16)
            nc.scalar.activation(a_tab[:, :, 0, :, :], a_f32, ACT.Copy)
            nc.scalar.activation(wres[:, 0, :], wres_f32, ACT.Copy).then_inc(S["setup_act"], 1)
            act.wait_ge(S["gdom_in"], 16)
            act.wait_ge(S["setup_dve"], 3)

            def body(t, on):
                j = t - 11
                for u in range(U):
                    if lagged(on, u, 2):
                        c, b = chunk(t, u, 2), (u - 2) % U
                        act.wait_ge(S["sub_done"], c + 1)
                        nc.scalar.activation(e_sb[0:TOK, b, :], e_sb[0:TOK, b, :], ACT.Exp).then_inc(S["e_exp"], 1)
                    if "xt" in on and u == 1:
                        act.wait_ge(S["x_in"], (t + 1) * 32)
                        ge(act, S["xt_mm"], t * 3)
                        nc.scalar.activation(xint[0:NP, :, :, :].rearrange("p f s e -> p s f e"), xin[0:NP, :, :, :],
                                             ACT.Copy).then_inc(S["xc_done"], 1)
                    if "ln" in on and u == 2:
                        k = t - 12
                        act.wait_ge(S["c_done"], k + 1)
                        ge(act, S["lsq_done"], k)
                        nc.scalar.activation(sq_sb[0:NP, :, :, :].rearrange("p s f e -> p (s f e)"),
                                             c_sb[0:NP, :, :, :].rearrange("p s f e -> p (s f e)"), ACT.Square
                                             ).then_inc(S["sq_done"], 1)
                    if lagged(on, u, 4):
                        c, b = chunk(t, u, 4), BUF3[(u - 4) % U]
                        act.wait_ge(S["pt_mm"], c + 1)
                        ge(act, S["av_mm"], c - AGO3[(u - 4) % U] + 1)
                        nc.scalar.activation(pt_sb[0:TOK, b, :], ps_pt[0:TOK, 0:W], ACT.Copy).then_inc(S["pt_ev"], 1)
                    if "front" in on:
                        c, b = chunk(t, u), BUF3[u]
                        act.wait_ge(S["t_mm"], c + 1)
                        ge(act, S["s_mm"], c - AGO3[u] + 1)
                        nc.scalar.activation(t_sb[:, b, :, :, :],
                                             ps_t[:, 0:W].rearrange("p (h q i) -> p q h i", h=H, q=PC),
                                             ACT.Copy).then_inc(S["t_ev"], 1)
                    if lagged(on, u, -1):
                        c = chunk(t, u, -1)
                        off = c % (U * ITS * 2) * PC
                        if u == U - 1 and "xt_on" in on:
                            act.wait_ge(S["xt_ev"], (t + 1) * 3)
                        ge(act, S["rt_mm"], c)
                        nc.scalar.activation(xh[:, :, :], xt[:, :, bass.ds(off, PC)], ACT.Copy
                                             ).then_inc(S["xh_done"], 1)
                    if "front" in on:
                        c, b = chunk(t, u), BUF3[u]
                        ge(act, S["s_mm"], c - AGO3[u] + 1)
                        ge(act, S["v_mm"], c - AGO3[u] + 1)
                        off = c % (U * ITS * 2) * PC
                        nc.scalar.activation(xbd[E:P, b, :, 1, :].rearrange("p q f -> p f q"),
                                             xt[E:P, :, bass.ds(off, PC)], ACT.Copy).then_inc(S["xbd1_done"], 1)
                    if lagged(on, u, 1):
                        c, b = chunk(t, u, 1), (u - 1) % U
                        act.wait_ge(S["v_mm"], c + 1)
                        ge(act, S["av_mm"], c - 4)
                        for s in range(2):
                            last = nc.scalar.activation(
                                vbd[0:TOK, b, :, :, s, :],
                                ps_v[0:TOK, 0:PC * E].rearrange("p (q h d) -> p q h d", q=PC, h=H),
                                ACT.Copy, scale=vmask[0:TOK, s:s + 1])
                        last.then_inc(S["v_ev"], 1)
                    if "front" in on:
                        c = chunk(t, u)
                        act.wait_ge(S["rt_mm"], c + 1)
                        ge(act, S["y_add"], c - 4)
                        nc.scalar.activation(rt_sb[:, u, :, :].rearrange("p f q -> p (f q)"), ps_rt[:, 0:HW_],
                                             ACT.Copy).then_inc(S["rt_ev"], 1)
                    if "xt" in on and 1 <= u <= 3:
                        f0, nf = XT_LUMPS[u - 1]
                        act.wait_ge(S["xt_mm"], t * 3 + u)
                        if "lag" in on and u == 1:
                            act.wait_ge(S["xh_done"], (t - 5) * U)
                            act.wait_ge(S["xl_done"], (t - 5) * U)
                            act.wait_ge(S["xbd0_done"], (t - 5) * U)
                            act.wait_ge(S["xbd1_done"], (t - 5) * U)
                        nc.scalar.activation(
                            xt[:, bass.ds(t % ITS * FI + f0, nf), bass.ds(t // ITS % 2 * NP, NP)],
                            ps_xt[:, 0:nf * NP].rearrange("p (f q) -> p f q", f=nf), ACT.Copy
                        ).then_inc(S["xt_ev"], 1)
                    if "bk" in on and u >= 2:
                        f0, nf = BK_LUMPS[u - 2]
                        act.wait_ge(S["bk_mm"], j * 3 + u - 1)
                        if u == 2:
                            ge(act, S["c_done"], j)
                        nc.scalar.activation(
                            r_sb[0:NP, :, f0:f0 + nf, :],
                            ps_bk[0:NP, 0:nf * P].rearrange("p (f s e) -> p s f e", f=nf, s=2),
                            ACT.Relu).then_inc(S["bk_ev"], 1)

            over(act, {"first": (0, 1), "xt": XT, "xt_on": (0, NI), "pre": PRE, "front": FRONT, "seventh": (6, 7),
                       "lag": LAG, "bk": BK, "ln": LN, "first ln": (12, 13)}, body)

        @block.tensor
        def _(pe):
            pe.wait_ge(S["setup_pool"], 2)
            pe.wait_ge(S["samp"], 1)
            nc.tensor.matmul(ps_s[:, 0:D], upper, tot, start=True, stop=True)
            nc.tensor.matmul(ps_s[:, D:2 * D], ones[:, 0:P], tot, start=True, stop=True).then_inc(S["cnt_ps"], 1)

            def place(i, first, stop):
                for b in range(OHB):
                    pe.wait_ge(S["oh_done"], i * OHB + b + 1)
                    nc.tensor.matmul(ps_av[:, 0:2 * NBLK], oh_p[b], oh_ns[b], start=first and b == 0,
                                     stop=stop and b == OHB - 1).then_inc(S["perm_mm"], 1)

            place(0, True, False)
            with pe.Fori(1, C // OHB - 1) as i:
                place(i, False, False)
            place(C // OHB - 1, False, True)
            pe.wait_ge(S["setup_dve"], 2)
            pe.wait_ge(S["w_in"], 16)
            pe.wait_ge(S["wk_in_s"], 16)
            for d in range(D):
                nc.tensor.transpose(ps_t[0:E, d * E:(d + 1) * E], wq_in[:, d, :], ident[0:E, 0:E])
            nc.tensor.transpose(ps_pt[0:E, 0:E], wk_in, ident[0:E, 0:E]).then_inc(S["wt_ps"], 1)
            pe.wait_ge(S["act_c"], 2)
            for d in range(D):
                if d >= 2:
                    pe.wait_ge(S["act_c"], d + 1)
                for s in range(2):
                    for h in range(H):
                        r = slice(h * HD, (h + 1) * HD)
                        last = nc.tensor.matmul(a_banks[d % 2][h][s * E:(s + 1) * E, 0:E], wqt[r, d, :], wkt[r, :],
                                                start=True, stop=True)
                last.then_inc(S["a_ps"], 1)
            pe.wait_ge(S["setup_dve"], 3)

            def body(t, on):
                j = t - 11
                for u in range(U):
                    if "front" in on:
                        c = chunk(t, u)
                        b = BUF3[u]
                        pe.wait_ge(S["xh_done"], c + 1)
                        pe.wait_ge(S["xl_done"], c + 1)
                        pe.wait_ge(a_in[b], ((t - 5) * NB3[b] + BUF3[:u + 1].count(b)) * 32)
                        ge(pe, S["t_ev"], c)
                        for h in range(H):
                            for i, (al, xp) in enumerate(PARTS):
                                last = nc.tensor.matmul(ps_t[:, h * HW_:(h + 1) * HW_],
                                                        a_sb[:, b, al, h, :, :].rearrange("p s e -> p (s e)"),
                                                        (xh, xl)[xp][:, :, :].rearrange("p f q -> p q f"),
                                                        start=i == 0, stop=i == len(PARTS) - 1)
                        last.then_inc(S["t_mm"], 1)
                        ge(pe, S["rt_ev"], c)
                        for i, (al, xp) in enumerate(PARTS):
                            last = nc.tensor.matmul(ps_rt[:, 0:HW_], wres[:, al, :],
                                                    (xh, xl)[xp][:, :, :].rearrange("p f q -> p (f q)"),
                                                    start=i == 0, stop=i == len(PARTS) - 1)
                        last.then_inc(S["rt_mm"], 1)
                    if lagged(on, u, 1):
                        c, b = chunk(t, u, 1), BUF3[(u - 1) % U]
                        pe.wait_ge(S["t_ev"], c + 1)
                        pe.wait_ge(S["xbd0_done"], c + 1)
                        pe.wait_ge(S["xbd1_done"], c + 1)
                        ge(pe, S["sub_done"], c)
                        for q in range(PC):
                            last = nc.tensor.matmul(
                                ps_s[0:TOK, q * TOK:(q + 1) * TOK],
                                t_sb[:, b, q, :, :].rearrange("p h i -> p (h i)"),
                                xbd[:, b, q, :, :].rearrange("p s j -> p (s j)"), start=True, stop=True)
                        last.then_inc(S["s_mm"], 1)
                    if lagged(on, u, 1):
                        c, b = chunk(t, u, 1), BUF3[(u - 1) % U]
                        ge(pe, S["v_ev"], c)
                        for q in range(PC):
                            last = nc.tensor.matmul(ps_v[0:TOK, q * E:(q + 1) * E],
                                                    xbd[:, b, q, :, :].rearrange("p s j -> p (s j)"), wv[:, :],
                                                    start=True, stop=True)
                        last.then_inc(S["v_mm"], 1)
                    if "xt" in on and 1 <= u <= 3:
                        f0, nf = XT_LUMPS[u - 1]
                        if u == 1:
                            pe.wait_ge(S["xc_done"], t + 1)
                        ge(pe, S["xt_ev"], t * 3 + u - 1)
                        for f in range(nf):
                            last = nc.tensor.transpose(ps_xt[:, f * NP:(f + 1) * NP],
                                                       xint[0:NP, f0 + f, :, :].rearrange("p s e -> p (s e)"),
                                                       ident[0:NP, 0:NP])
                        last.then_inc(S["xt_mm"], 1)
                    if "bk" in on and u >= 2:
                        f0, nf = BK_LUMPS[u - 2]
                        if u == 2:
                            pe.wait_ge(S["y_in"], (j + 1) * 16)
                        ge(pe, S["bk_ev"], j * 3 + u - 2)
                        for f in range(nf):
                            last = nc.tensor.transpose(ps_bk[0:NP, f * P:(f + 1) * P], yst[:, f0 + f, :],
                                                       perm_id[:, :])
                        last.then_inc(S["bk_mm"], 1)
                    if lagged(on, u, 3):
                        c, b = chunk(t, u, 3), (u - 3) % U
                        pe.wait_ge(S["e_norm"], c + 1)
                        ge(pe, S["pt_ev"], c)
                        for q in range(PC):
                            last = nc.tensor.transpose(ps_pt[0:TOK, q * TOK:(q + 1) * TOK],
                                                       e_sb[0:TOK, b, q * TOK:(q + 1) * TOK], ident[0:TOK, 0:TOK])
                        last.then_inc(S["pt_mm"], 1)
                    if lagged(on, u, 4):
                        c, b = chunk(t, u, 4), (u - 4) % U
                        pe.wait_ge(S["pt_ev"], c + 1)
                        pe.wait_ge(S["v_ev"], c + 1)
                        ge(pe, S["y_add"], c)
                        for q in range(PC):
                            last = nc.tensor.matmul(
                                ps_av[:, q * TOK:(q + 1) * TOK],
                                vbd[0:TOK, b, q, :, :, :].rearrange("p h s d -> p (h s d)"),
                                pt_sb[0:TOK, BUF3[b], q * TOK:(q + 1) * TOK], start=True, stop=True)
                        last.then_inc(S["av_mm"], 1)

            over(pe, {"first": (0, 1), "seventh": (6, 7), "xt": XT, "front": FRONT, "lag": LAG, "bk": BK,
                      "first bk": (11, 12)}, body)


_ARGS = [("r_inputs", "x"), ("r_domain_ids", "ids"), ("L0_rec_W_Query_domains", "w_q"), ("L0_rec_W_key", "w_k"),
         ("L0_rec_W_Value", "w_v"), ("L0_rec_W_Res", "w_res"), ("L0_rec_ln_scale", "ln_scale"),
         ("L0_rec_ln_bias", "ln_bias")]


def kernel(**inputs):
    import numpy as np
    import concourse.bacc as bacc
    from concourse.bass_utils import run_bass_kernel_spmd

    nc = bacc.Bacc("TRN2", target_bir_lowering=False, num_devices=1)
    arrays, args = {}, {}
    for name, short in _ARGS:
        a = np.ascontiguousarray(inputs[name])
        arrays[f"in_{short}"] = a
        args[short] = nc.dram_tensor(f"in_{short}", a.shape, mybir.dt.from_np(a.dtype), kind="ExternalInput").ap()
    shape = arrays["in_x"].shape
    args["out"] = nc.dram_tensor("out_y", shape, F32, kind="ExternalOutput").ap()
    build(nc, **args)
    r = run_bass_kernel_spmd(nc, [arrays], core_ids=[0])
    return r.results[0]["out_y"]
```
